# Optimizing a Trainium2 kernel written in Bass

```python
import numpy as np
import jax
import jax.numpy as jnp

def _softmax(x, axis=-1):
    return jax.nn.softmax(x, axis=axis)

def _gelu(x):
    return jax.nn.gelu(x, approximate=True)

def _silu(x):
    return jax.nn.silu(x)

def _sigmoid(x):
    return jax.nn.sigmoid(x)

def _layernorm(x, axis=-1, eps=1e-05):
    m = jnp.mean(x, axis=axis, keepdims=True)
    v = jnp.var(x, axis=axis, keepdims=True)
    return (x - m) / jnp.sqrt(v + eps)

def _scatter_add(tgt, idx, src, axis=0):
    return tgt.at[idx].add(src)

def _segment_sum(src, seg, n):
    return jax.ops.segment_sum(src, seg, n)
kernel_name = 'mk_dlrm_tower_d1_rec_r8_432acd'

def setup_inputs(seed: int=0):
    np.random.seed(seed)
    _w = jnp.asarray

    def _rec_inputs():
        import jax
        import jax.numpy as jnp
        _tk = jax.random.key(seed)
        ids = jnp.stack([jax.random.randint(jax.random.fold_in(_tk, 200 + f), (2048,), 0, v, jnp.int32) for f, v in enumerate([12500, 1250, 12500, 1000, 125000, 12500, 1250, 1250, 1250, 1000, 12500, 1250, 1000, 1250, 1000, 1250, 12500, 12500, 1000, 1250, 1000, 1250, 1000, 1250, 1000, 1250])], axis=1)
        tbl_0 = 0.05 * jax.random.normal(jax.random.fold_in(_tk, 500 + 0), (12500, 128), jnp.float32)
        tbl_1 = 0.05 * jax.random.normal(jax.random.fold_in(_tk, 500 + 1), (1250, 128), jnp.float32)
        tbl_2 = 0.05 * jax.random.normal(jax.random.fold_in(_tk, 500 + 2), (12500, 128), jnp.float32)
        tbl_3 = 0.05 * jax.random.normal(jax.random.fold_in(_tk, 500 + 3), (1000, 128), jnp.float32)
        tbl_4 = 0.05 * jax.random.normal(jax.random.fold_in(_tk, 500 + 4), (125000, 128), jnp.float32)
        tbl_5 = 0.05 * jax.random.normal(jax.random.fold_in(_tk, 500 + 5), (12500, 128), jnp.float32)
        tbl_6 = 0.05 * jax.random.normal(jax.random.fold_in(_tk, 500 + 6), (1250, 128), jnp.float32)
        tbl_7 = 0.05 * jax.random.normal(jax.random.fold_in(_tk, 500 + 7), (1250, 128), jnp.float32)
        tbl_8 = 0.05 * jax.random.normal(jax.random.fold_in(_tk, 500 + 8), (1250, 128), jnp.float32)
        tbl_9 = 0.05 * jax.random.normal(jax.random.fold_in(_tk, 500 + 9), (1000, 128), jnp.float32)
        tbl_10 = 0.05 * jax.random.normal(jax.random.fold_in(_tk, 500 + 10), (12500, 128), jnp.float32)
        tbl_11 = 0.05 * jax.random.normal(jax.random.fold_in(_tk, 500 + 11), (1250, 128), jnp.float32)
        tbl_12 = 0.05 * jax.random.normal(jax.random.fold_in(_tk, 500 + 12), (1000, 128), jnp.float32)
        tbl_13 = 0.05 * jax.random.normal(jax.random.fold_in(_tk, 500 + 13), (1250, 128), jnp.float32)
        tbl_14 = 0.05 * jax.random.normal(jax.random.fold_in(_tk, 500 + 14), (1000, 128), jnp.float32)
        tbl_15 = 0.05 * jax.random.normal(jax.random.fold_in(_tk, 500 + 15), (1250, 128), jnp.float32)
        tbl_16 = 0.05 * jax.random.normal(jax.random.fold_in(_tk, 500 + 16), (12500, 128), jnp.float32)
        tbl_17 = 0.05 * jax.random.normal(jax.random.fold_in(_tk, 500 + 17), (12500, 128), jnp.float32)
        tbl_18 = 0.05 * jax.random.normal(jax.random.fold_in(_tk, 500 + 18), (1000, 128), jnp.float32)
        tbl_19 = 0.05 * jax.random.normal(jax.random.fold_in(_tk, 500 + 19), (1250, 128), jnp.float32)
        tbl_20 = 0.05 * jax.random.normal(jax.random.fold_in(_tk, 500 + 20), (1000, 128), jnp.float32)
        tbl_21 = 0.05 * jax.random.normal(jax.random.fold_in(_tk, 500 + 21), (1250, 128), jnp.float32)
        tbl_22 = 0.05 * jax.random.normal(jax.random.fold_in(_tk, 500 + 22), (1000, 128), jnp.float32)
        tbl_23 = 0.05 * jax.random.normal(jax.random.fold_in(_tk, 500 + 23), (1250, 128), jnp.float32)
        tbl_24 = 0.05 * jax.random.normal(jax.random.fold_in(_tk, 500 + 24), (1000, 128), jnp.float32)
        tbl_25 = 0.05 * jax.random.normal(jax.random.fold_in(_tk, 500 + 25), (1250, 128), jnp.float32)
        _rk = jax.random.fold_in(_tk, 7)
        r_dense_output = -0.000520686 + 1.00062 * jax.random.normal(jax.random.fold_in(_rk, 101), (2048, 128), jnp.float32)
        W_top1 = 0.0405887 * jax.random.normal(jax.random.fold_in(_tk, 801), (607, 512), jnp.float32)
        W_top2 = 0.0441942 * jax.random.normal(jax.random.fold_in(_tk, 802), (512, 256), jnp.float32)
        W_top3 = 0.0625 * jax.random.normal(jax.random.fold_in(_tk, 803), (256, 1), jnp.float32)
        b_top1 = jnp.zeros((512,), jnp.float32)
        b_top2 = jnp.zeros((256,), jnp.float32)
        return (r_dense_output, ids, tbl_0, tbl_1, tbl_2, tbl_3, tbl_4, tbl_5, tbl_6, tbl_7, tbl_8, tbl_9, tbl_10, tbl_11, tbl_12, tbl_13, tbl_14, tbl_15, tbl_16, tbl_17, tbl_18, tbl_19, tbl_20, tbl_21, tbl_22, tbl_23, tbl_24, tbl_25, W_top1, b_top1, W_top2, b_top2, W_top3)
    r_dense_output, ids, tbl_0, tbl_1, tbl_2, tbl_3, tbl_4, tbl_5, tbl_6, tbl_7, tbl_8, tbl_9, tbl_10, tbl_11, tbl_12, tbl_13, tbl_14, tbl_15, tbl_16, tbl_17, tbl_18, tbl_19, tbl_20, tbl_21, tbl_22, tbl_23, tbl_24, tbl_25, W_top1, b_top1, W_top2, b_top2, W_top3 = _rec_inputs()

    def _L0_rec_setup():
        import jax, jax.numpy as jnp
        import numpy as np
        B, NUM_SPARSE, D = (2048, 26, 128)
        key = jax.random.key(seed)
        k1, k2 = jax.random.split(key)
        dense_output = jax.random.normal(k1, (B, D), dtype=jnp.float32)
        embeddings = jax.random.normal(k2, (B, NUM_SPARSE, D), dtype=jnp.float32)
        return {'dense_output': dense_output, 'embeddings': embeddings}
    _L0_rec_all = _L0_rec_setup()
    _L0_rec_in = {k: v for k, v in _L0_rec_all.items() if k in ()}
    del _L0_rec_all
    return {'r_dense_output': r_dense_output, 'ids': ids, 'tbl_0': tbl_0, 'tbl_1': tbl_1, 'tbl_2': tbl_2, 'tbl_3': tbl_3, 'tbl_4': tbl_4, 'tbl_5': tbl_5, 'tbl_6': tbl_6, 'tbl_7': tbl_7, 'tbl_8': tbl_8, 'tbl_9': tbl_9, 'tbl_10': tbl_10, 'tbl_11': tbl_11, 'tbl_12': tbl_12, 'tbl_13': tbl_13, 'tbl_14': tbl_14, 'tbl_15': tbl_15, 'tbl_16': tbl_16, 'tbl_17': tbl_17, 'tbl_18': tbl_18, 'tbl_19': tbl_19, 'tbl_20': tbl_20, 'tbl_21': tbl_21, 'tbl_22': tbl_22, 'tbl_23': tbl_23, 'tbl_24': tbl_24, 'tbl_25': tbl_25, 'W_top1': W_top1, 'b_top1': b_top1, 'W_top2': W_top2, 'b_top2': b_top2, 'W_top3': W_top3}

def reference(r_dense_output, ids, tbl_0, tbl_1, tbl_2, tbl_3, tbl_4, tbl_5, tbl_6, tbl_7, tbl_8, tbl_9, tbl_10, tbl_11, tbl_12, tbl_13, tbl_14, tbl_15, tbl_16, tbl_17, tbl_18, tbl_19, tbl_20, tbl_21, tbl_22, tbl_23, tbl_24, tbl_25, W_top1, b_top1, W_top2, b_top2, W_top3):
    import jax
    import jax.numpy as jnp

    def _L0_rec_ref(dense_output, embeddings):
        import jax, jax.numpy as jnp
        import numpy as np
        B, NUM_SPARSE, D = (2048, 26, 128)
        combined = jnp.concatenate([dense_output[:, None, :], embeddings], axis=1)
        interactions = jnp.einsum('bfd,bgd->bfg', combined, combined)
        F = combined.shape[1]
        iu, ju = jnp.triu_indices(F, k=1)
        interactions_flat = interactions[:, iu, ju]
        return jnp.concatenate([dense_output, interactions_flat], axis=1)
    e = jnp.stack([tbl_0[ids[:, 0]], tbl_1[ids[:, 1]], tbl_2[ids[:, 2]], tbl_3[ids[:, 3]], tbl_4[ids[:, 4]], tbl_5[ids[:, 5]], tbl_6[ids[:, 6]], tbl_7[ids[:, 7]], tbl_8[ids[:, 8]], tbl_9[ids[:, 9]], tbl_10[ids[:, 10]], tbl_11[ids[:, 11]], tbl_12[ids[:, 12]], tbl_13[ids[:, 13]], tbl_14[ids[:, 14]], tbl_15[ids[:, 15]], tbl_16[ids[:, 16]], tbl_17[ids[:, 17]], tbl_18[ids[:, 18]], tbl_19[ids[:, 19]], tbl_20[ids[:, 20]], tbl_21[ids[:, 21]], tbl_22[ids[:, 22]], tbl_23[ids[:, 23]], tbl_24[ids[:, 24]], tbl_25[ids[:, 25]]], axis=1)
    z = _L0_rec_ref(r_dense_output, e)
    z = z.reshape(z.shape[0], -1)
    h = jnp.concatenate([z, r_dense_output], axis=1)
    h = jnp.maximum(h @ W_top1 + b_top1, 0.0)
    h = jnp.maximum(h @ W_top2 + b_top2, 0.0)
    y = h @ W_top3
    return y

_drawn_inputs = setup_inputs


def setup_inputs(seed=0):
    import zlib

    import numpy as np

    out = dict(_drawn_inputs(seed))
    spreads = {'b_top1': (0.0, 0.1), 'b_top2': (0.0, 0.1)}
    factors = {}
    for name, (base, spread) in spreads.items():
        noise = np.random.default_rng([zlib.crc32(name.encode()), seed]).standard_normal(out[name].shape)
        drawn = base * np.exp(spread * noise) if base else spread * noise
        out[name] = jnp.asarray(drawn.astype(out[name].dtype))
    for name, factor in factors.items():
        out[name] = (out[name] * factor).astype(out[name].dtype)
    return out
```

```python
import concourse.bass as bass
from concourse import mybir
from contextlib import ExitStack

P = 128
D = 128
GROUP = 4
SPAN = P // GROUP
TILES = 4
ONE_HOT_ROWS = 1000


def dlrm_program(nc, dense, gather_idx, one_hot_idx, gathered, small, W1_dense, W1_pairs, b1, W2,
                 b2, w3, out):
    f32, f32r, i32 = mybir.dt.float32, mybir.dt.float32r, mybir.dt.int32
    ALU = mybir.AluOpType
    ACT = mybir.ActivationFunctionType

    batch = out.shape[0]
    SUPERS = batch // (TILES * P)
    LAST = SUPERS - 1
    N = TILES * P
    PAIR_N = 2 * P
    NG = len(gathered)
    NS = len(small)
    F = 1 + NG + NS
    NE = 1 + NG
    HALF = F // 2
    FEXT = F + HALF
    F_BLOCK = 9
    PITCH = HALF + 1
    PAIR_ROWS = F_BLOCK * PITCH
    KP = F // F_BLOCK
    H1, H2 = W1_dense.shape[-1], W2.shape[-1]
    M1, M2 = H1 // P, H2 // P
    T_BANKS = -(-NE // 4)
    C_BANKS = -(-(FEXT - 1) // 4)
    GROUPS = P // GROUP
    G_SIZE = 8
    G_FILLS = GROUPS // G_SIZE
    G_COLS = GROUP * F
    ROWS_K = 8
    ROWS_P = ONE_HOT_ROWS // ROWS_K
    CHUNK_K = 4
    OH_TABLES = NS // 2
    OH_CHUNKS = OH_TABLES * ROWS_K // CHUNK_K
    OH_RING = 2
    OH_FILLS = OH_TABLES // 2

    ctx = ExitStack()
    with ctx:
        def sb(name, shape, dt):
            return ctx.enter_context(nc.sbuf_tensor(name, shape, dt))

        def pb(name, shape, dt):
            return ctx.enter_context(nc.psum_tensor(name, shape, dt))

        def sem(name):
            return ctx.enter_context(nc.semaphore(name))

        def sems(name, n):
            return [sem(f"{name}{i}") for i in range(n)]

        E = sb("E", [P, 2, NE, D], f32)
        ET = sb("ET", [P, TILES, P, SPAN], f32)
        tab_hi = sb("tab_hi", [P, NS, ROWS_K, D], f32r)
        tab_lo = sb("tab_lo", [P, NS, ROWS_K, D], f32r)
        one_hot = sb("one_hot", [P, OH_RING, CHUNK_K, PAIR_N], f32r)
        gidx = sb("gidx", [P, TILES, NG], i32)
        oidx = sb("oidx", [P, 2, OH_TABLES, PAIR_N], i32)
        row_id = sb("row_id", [P, ROWS_K], i32)
        ident = sb("ident", [P, P], f32)
        S = sb("S", [P, P, F], f32)
        UH = sb("UH", [P, M1 * N], f32)
        U = UH[:, 0:GROUP * F * PITCH].rearrange("p (s r) -> p s r", s=GROUP)
        h1 = UH[:, :].rearrange("p (m n) -> p m n", m=M1)
        ZH = sb("ZH", [P, KP * N], f32)
        Zp = ZH[:, :].rearrange("p (k n) -> p k n", k=KP)
        h2 = ZH[:, 0:M2 * N].rearrange("p (m n) -> p m n", m=M2)
        Zd = sb("Zd", [P, GROUP, P], f32)
        w1d = sb("w1d", [P, H1], f32)
        w1p = sb("w1p", [PAIR_ROWS, KP, H1], f32)
        w2 = sb("w2", [P, M1, H2], f32)
        w3s = sb("w3s", [P, M2], f32)
        b1s = sb("b1s", [P, M1], f32)
        b2s = sb("b2s", [P, M2], f32)
        credit = sb("credit", [1, 2], f32)
        Y = sb("Y", [P, SUPERS * GROUP], f32)

        psT = [pb(f"psT{i}", [P, 512], f32) for i in range(2)]
        psM = [pb(f"psM{i}", [P, 512], f32) for i in range(2)]
        psG = [pb(f"psG{i}", [P, 2, 512], f32) for i in range(2)]

        raw_tables = ET[:, 2:4].rearrange("p q n f -> p (q n f)")

        def raw_table(h):
            return raw_tables[0:ROWS_P, h * ROWS_K * D:(h + 1) * ROWS_K * D]

        raw_w1d = UH[:, 0:2 * H1].rearrange("p (a n) -> p a n", a=2)

        gidx_in = sems("gidx_in", TILES)
        dense_in = sems("dense_in", 2)
        oidx_in = sems("oidx_in", 2)
        table_in = sems("table_in", NS)
        w1d_in, weights_in = sem("w1d_in"), sem("weights_in")
        gathered_in = sems("gathered_in", 2)
        zeroed, ident_ready, row_id_ready = sem("zeroed"), sem("ident_ready"), sem("row_id_ready")
        pad_ready, hi_ready, lo_ready, w1d_ready = (sem("pad_ready"), sem("hi_ready"),
                                                    sem("lo_ready"), sem("w1d_ready"))
        E_free = sems("E_free", TILES)
        T_full = sems("T_full", 2)
        T_out = sems("T_out", 2)
        M_out = sems("M_out", 2)
        L_full = sems("L_full", 2)
        G_full = sems("G_full", 2)
        G_out_act, G_out_dve = sems("G_out_act", 2), sems("G_out_dve", 2)
        hot_full, hot_used = sems("hot_full", OH_RING), sems("hot_used", OH_RING)

        def e_freed(u, q):
            return 16 * (u + 1 + (q + 2) // TILES)

        FIRST, MIDDLE, LAST_ONE, END = range(4)
        PARTS = M1 + M2 + 1
        FILL_CHUNKS = OH_CHUNKS // OH_FILLS

        def has_hot_slot(kind, q):
            return not (kind == LAST_ONE and q >= 2)

        def between(steps, inserted, every):
            merged = []
            for i, step in enumerate(steps):
                merged.append(step)
                if (i + 1) % every == 0 and inserted:
                    merged.append(inserted[0])
                    inserted = inserted[1:]
            return merged + inserted

        def steps_of(kind, q):
            turn = [("C", b) for b in range(C_BANKS)], [("K", k) for k in range(KP)]
            if kind == END:
                return turn[0] + turn[1] + [("part", p) for p in range(PARTS)]
            tile = [("T", b) for b in range(T_BANKS)]
            hot = [("hot", c) for c in range(OH_CHUNKS)] if has_hot_slot(kind, q) else []
            grams = [("gram", i) for i in range(G_FILLS)]
            parts = [("part", p) for p in range(2 * q, min(2 * q + 2, PARTS))]
            if kind == FIRST:
                return tile[:1] + between(tile[1:], hot[:FILL_CHUNKS], 1) + between(
                    grams, hot[FILL_CHUNKS:], 1)
            if q == 0:
                return between(turn[0] + tile + turn[1], hot, 2) + between(grams, parts, 2)
            return tile[:1] + between(tile[1:], hot[:FILL_CHUNKS], 1) + parts[:1] + between(
                grams[:3], parts[1:], 2) + between(grams[3:], hot[FILL_CHUNKS:], 1)

        def tiles_of(kind):
            return range(1 if kind == END else TILES)

        def T_fills(kind):
            return [(step, q, i) for q in tiles_of(kind) for step, i in steps_of(kind, q)
                    if step in ("T", "C", "K")]

        def M_fills(kind):
            return [(step, q, i) for q in tiles_of(kind) for step, i in steps_of(kind, q)
                    if step == "part" or (step == "hot" and i % FILL_CHUNKS == 0)]

        def bank_of(fills, kind, fill):
            return fills(kind).index(fill) % 2

        def signals_T_full(fill):
            return fill[0] != "T" or fill[2] < T_BANKS - 1

        def fills_before(fills, u, kind, fill, counted=lambda fill: True):
            i = fills(kind).index(fill)

            def count(sequence):
                return sum(1 for other in sequence[i % 2::2] if counted(other))

            before = 0
            if kind != FIRST:
                before = count(fills(FIRST)) + (u - 1) * count(fills(MIDDLE))
            if kind == END:
                before = before + count(fills(LAST_ONE))
            return before + count(fills(kind)[:i])

        def t_bank(kind, fill):
            return bank_of(T_fills, kind, fill)

        def t_uses(u, kind, fill):
            return fills_before(T_fills, u, kind, fill)

        def t_signals(u, kind, fill):
            return fills_before(T_fills, u, kind, fill, signals_T_full)

        def m_bank(kind, fill):
            return bank_of(M_fills, kind, fill)

        def m_uses(u, kind, fill):
            return OH_FILLS + fills_before(M_fills, u, kind, fill)

        def tile_of_part(kind, part):
            return 0 if kind == END else part // 2

        def l_fills(v, part):
            return (PARTS + 1 - part % 2) // 2 * v + part // 2

        def g_uses(u, q, i):
            return (TILES * u + q) * (G_FILLS // 2) + i // 2

        def hot_uses(n, c):
            return n * (OH_CHUNKS // OH_RING) + c // OH_RING

        def hot_slot(u, q):
            return TILES * u + q + 2

        def rows_of(kp):
            return PAIR_ROWS - (1 if kp == KP - 1 else 0)

        block = ctx.enter_context(nc.Block())

        @block.gpsimd
        def _(pool):
            nc.gpsimd.iota(row_id[:, :], pattern=[[1, ROWS_K]], base=0,
                           channel_multiplier=ROWS_K).then_inc(row_id_ready, 1)
            nc.gpsimd.memset(ident[:, :], 0.0).then_inc(zeroed, 1)
            for q in range(2):
                nc.gpsimd.memset(credit[:, q:q + 1], 0.0).then_inc(E_free[q], 16)
            pool.wait_ge(zeroed, 1)
            nc.gpsimd.affine_select(out=ident[:, :], in_=ident[:, :], compare_op=ALU.not_equal,
                                    fill=1.0, base=0, pattern=[[-1, P]],
                                    channel_multiplier=1).then_inc(ident_ready, 1)

            def super_tile(loads):
                for q in range(TILES):
                    pool.wait_ge(ident_ready, 1)
                    pool.wait_ge(gidx_in[q], loads)
                    pool.wait_ge(E_free[q], loads)
                    for g in range(NG):
                        pool.indirect_dma_start(
                            E[:, q % 2, 1 + g, :], None, gathered[g],
                            bass.IndirectOffsetOnAxis(ap=gidx[:, q, g:g + 1], axis=0),
                        ).then_inc(gathered_in[q % 2], 16)

            with pool.Fori(16, 16 * (SUPERS + 1), 16) as loads:
                super_tile(loads)

        @block.sync
        def _(sp):
            def load_gidx(u, q):
                sp.dma_start(gidx[:, q, :], gather_idx[u * TILES + q]).then_inc(gidx_in[q], 16)

            def load_dense(tile, slot):
                sp.dma_start(E[:, slot, 0, :], dense[tile]).then_inc(dense_in[slot], 16)

            def load_oidx(n, half):
                sp.dma_start(oidx[:, half].rearrange("p t n -> p (t n)"),
                             one_hot_idx[n].partition_broadcast(P)).then_inc(oidx_in[half], 16)

            load_gidx(0, 0)
            load_oidx(0, 0)
            for h in range(NS):
                sp.dma_start(raw_table(h), small[h].rearrange("(p k) d -> p (k d)", k=ROWS_K)
                             ).then_inc(table_in[h], 16)
                if h == 0:
                    for q in range(1, TILES):
                        load_gidx(0, q)
                    load_dense(0, 0)
                    load_dense(1, 1)
                    load_oidx(1, 1)
            sp.dma_start(raw_w1d, W1_dense.rearrange("a p n -> p a n")).then_inc(w1d_in, 16)
            sp.dma_start(w1p[:, :, :], W1_pairs.rearrange("(k p) n -> p k n", k=KP)).then_inc(weights_in, 16)
            sp.dma_start(w2[:, :, :], W2.rearrange("(k p) n -> p k n", p=P)).then_inc(weights_in, 16)
            sp.dma_start(b1s[:, :], b1).then_inc(weights_in, 16)
            sp.dma_start(b2s[:, :], b2).then_inc(weights_in, 16)
            sp.dma_start(w3s[:, :], w3).then_inc(weights_in, 16)

            def super_tile(u, kind):
                for q in range(TILES):
                    if has_hot_slot(kind, q):
                        sp.wait_ge(hot_full[OH_RING - 1], hot_uses(TILES * u + q + 1, 0))
                        load_oidx(hot_slot(u, q), q % 2)
                    if kind != LAST_ONE:
                        sp.wait_ge(gathered_in[q % 2], 16 * NG * (2 * u + q // 2 + 1))
                        load_gidx(u + 1, q)
                    if not (kind == LAST_ONE and q >= 2):
                        sp.wait_ge(E_free[(q + 2) % TILES], e_freed(u, q))
                        load_dense(TILES * u + q + 2, q % 2)

            with sp.Fori(0, LAST) as u:
                super_tile(u, MIDDLE)
            super_tile(LAST, LAST_ONE)
            y_fill = ("part", 0, PARTS - 1)
            sp.wait_ge(M_out[m_bank(END, y_fill)], m_uses(LAST, END, y_fill) + 1)
            sp.dma_start(out.rearrange("(p c) o -> p (c o)", p=P), Y[:, :]).then_inc(weights_in, 16)
            sp.wait_ge(weights_in, 16 * 6)

        @block.tensor
        def _(pe):
            def one_hot_chunk(n, half, chunk, bank, uses):
                if chunk % FILL_CHUNKS == 0:
                    pe.wait_ge(M_out[bank], uses)
                r = chunk % OH_RING
                t, c = chunk // (ROWS_K // CHUNK_K), chunk % (ROWS_K // CHUNK_K)
                pe.wait_ge(hot_full[r], hot_uses(n, chunk) + 1)
                for kc in range(CHUNK_K):
                    k = c * CHUNK_K + kc
                    for part, tab in enumerate((tab_hi, tab_lo)):
                        product = nc.tensor.matmul(
                            psM[bank][:, t % 2 * PAIR_N:(t % 2 + 1) * PAIR_N],
                            tab[0:ROWS_P, half * OH_TABLES + t, k, :],
                            one_hot[0:ROWS_P, r, kc, :],
                            start=(k == 0 and part == 0),
                            stop=(k == ROWS_K - 1 and part == 1))
                product.then_inc(hot_used[r], 1)

            def transpose_tile(u, kind, q, b):
                if b == 0:
                    pe.wait_ge(dense_in[q % 2], 16 * (2 * u + q // 2 + 1))
                    pe.wait_ge(gathered_in[q % 2], 16 * NG * (2 * u + q // 2 + 1))
                fill = ("T", q, b)
                bank = t_bank(kind, fill)
                pe.wait_ge(T_out[bank], t_uses(u, kind, fill))
                for f in range(4 * b, min(4 * b + 4, NE)):
                    turned = nc.tensor.transpose(psT[bank][:, (f % 4) * P:(f % 4 + 1) * P],
                                                 E[:, q % 2, f, :], ident[:, :])
                if b == T_BANKS - 1:
                    turned.then_inc(E_free[(q + 2) % TILES], 16)
                else:
                    turned.then_inc(T_full[bank], 1)

            def wait_ET(u, kind, q):
                for fill in (("T", q, T_BANKS - 2), ("T", q, T_BANKS - 1)):
                    pe.wait_ge(T_out[t_bank(kind, fill)], t_uses(u, kind, fill) + 1)
                if q == 0:
                    for fill in M_fills(kind)[0:2]:
                        pe.wait_ge(M_out[m_bank(kind, fill)], m_uses(u, kind, fill))
                if q == 2:
                    for fill in [fill for fill in M_fills(kind) if fill[1] == 1][-2:]:
                        pe.wait_ge(M_out[m_bank(kind, fill)], m_uses(u, kind, fill) + 1)

            def gram_fill(u, q, i):
                pe.wait_ge(G_out_act[i % 2], g_uses(u, q, i))
                pe.wait_ge(G_out_dve[i % 2], g_uses(u, q, i))
                for g in range(G_SIZE):
                    j = i * G_SIZE + g
                    four = ET[:, q, j * GROUP:(j + 1) * GROUP]
                    gram = nc.tensor.matmul(
                        psG[i % 2][:, g // 4, (g % 4) * G_COLS:(g % 4 + 1) * G_COLS],
                        four.rearrange("p s f -> p (s f)"), four[:, :, 0:F],
                        start=True, stop=True)
                gram.then_inc(G_full[i % 2], 1)

            def turn_columns(u, kind, b, v):
                if b == 0:
                    for i in range(2):
                        pe.wait_ge(G_out_act[i], g_uses(v, TILES, i))
                        pe.wait_ge(G_out_dve[i], g_uses(v, TILES, i))
                fill = ("C", 0, b)
                bank = t_bank(kind, fill)
                pe.wait_ge(T_out[bank], t_uses(u, kind, fill))
                for c in range(1 + 4 * b, min(5 + 4 * b, FEXT)):
                    turned = nc.tensor.transpose(psT[bank][:, (c - 1) % 4 * P:((c - 1) % 4 + 1) * P],
                                                 S[:, :, c % F], ident[:, :])
                turned.then_inc(T_full[bank], 1)

            def turn_pairs(u, kind, kp):
                if kp == 0:
                    for fill in (("C", 0, C_BANKS - 2), ("C", 0, C_BANKS - 1)):
                        pe.wait_ge(T_out[t_bank(kind, fill)], t_uses(u, kind, fill) + 1)
                fill = ("K", 0, kp)
                bank = t_bank(kind, fill)
                pe.wait_ge(T_out[bank], t_uses(u, kind, fill))
                for s in range(GROUP):
                    turned = nc.tensor.transpose(
                        psT[bank][0:rows_of(kp), s * P:(s + 1) * P],
                        U[:, s, kp * PAIR_ROWS:kp * PAIR_ROWS + rows_of(kp)], ident[:, :])
                turned.then_inc(T_full[bank], 1)

            def perceptron_part(u, kind, part, v):
                fill = ("part", tile_of_part(kind, part), part)
                bank = m_bank(kind, fill)
                pe.wait_ge(M_out[bank], m_uses(u, kind, fill))

                def written(other):
                    fill = ("part", tile_of_part(kind, other), other)
                    pe.wait_ge(M_out[m_bank(kind, fill)], m_uses(u, kind, fill) + 1)

                if part < M1:
                    cols = slice(part * P, (part + 1) * P)
                    if part == 0:
                        for kp in range(KP):
                            turned = ("K", 0, kp)
                            pe.wait_ge(T_out[t_bank(kind, turned)], t_uses(u, kind, turned) + 1)
                    nc.tensor.matmul(psM[bank][:, :], w1d[:, cols], Zd[:, :, :], start=True, stop=False)
                    for kp in range(KP):
                        layer = nc.tensor.matmul(psM[bank][:, :], w1p[0:rows_of(kp), kp, cols],
                                                 Zp[0:rows_of(kp), kp, :], start=False,
                                                 stop=(kp == KP - 1))
                elif part < M1 + M2:
                    cols = slice((part - M1) * P, (part - M1 + 1) * P)
                    for k in range(M1):
                        if part == M1:
                            written(k)
                        layer = nc.tensor.matmul(psM[bank][:, :], w2[:, k, cols], h1[:, k, :],
                                                 start=(k == 0), stop=(k == M1 - 1))
                else:
                    for k in range(M2):
                        written(M1 + k)
                    for s in range(GROUP):
                        for k in range(M2):
                            layer = nc.tensor.matmul(psM[bank][:, s:s + 1], h2[:, k, s * P:(s + 1) * P],
                                                     w3s[:, k:k + 1], start=(k == 0), stop=(k == M2 - 1))
                layer.then_inc(L_full[part % 2], 1)

            def super_tile(u, kind, v):
                for q in tiles_of(kind):
                    for step, i in steps_of(kind, q):
                        if step == "T":
                            transpose_tile(u, kind, q, i)
                        elif step == "hot":
                            fill = ("hot", q, i - i % FILL_CHUNKS)
                            one_hot_chunk(hot_slot(u, q), q % 2, i, m_bank(kind, fill),
                                          m_uses(u, kind, fill))
                        elif step == "gram":
                            if i == 0:
                                wait_ET(u, kind, q)
                            gram_fill(u, q, i)
                        elif step == "C":
                            turn_columns(u, kind, i, v)
                        elif step == "K":
                            turn_pairs(u, kind, i)
                        elif step == "part":
                            perceptron_part(u, kind, i, v)

            pe.wait_ge(ident_ready, 1)
            for half in range(2):
                for chunk in range(OH_CHUNKS):
                    if chunk % (ROWS_K // CHUNK_K) == 0:
                        pe.wait_ge(lo_ready, half * OH_TABLES + chunk // (ROWS_K // CHUNK_K) + 1)
                    one_hot_chunk(half, half, chunk, chunk // FILL_CHUNKS % 2, half)
            pe.wait_ge(pad_ready, 2)
            super_tile(0, FIRST, None)
            pe.wait_ge(weights_in, 16 * 5)
            pe.wait_ge(w1d_ready, 1)
            with pe.Fori(1, LAST) as u:
                super_tile(u, MIDDLE, u - 1)
            super_tile(LAST, LAST_ONE, LAST - 1)
            super_tile(LAST, END, LAST)

        def copy_out(eng, psum, sbuf):
            return nc.scalar.copy(sbuf, psum) if eng is nc.scalar else nc.vector.tensor_copy(sbuf, psum)

        ACT_GRAMS, DVE_GRAMS = (0, 1, 2), (3,)

        def empty_grams(eng, mine, done, u, q, i):
            eng.wait_ge(G_full[i % 2], g_uses(u, q, i) + 1)
            for s in mine:
                rows = slice(s * SPAN, (s + 1) * SPAN)
                blocks = psG[i % 2][rows, :, 0:4 * G_COLS].rearrange(
                    "p a (g c) -> p a g c", g=4)[:, :, :, s * F:(s + 1) * F]
                j0 = q * GROUPS + i * G_SIZE
                copied = copy_out(eng, blocks, S[rows, j0:j0 + G_SIZE, :].rearrange(
                    "p (a g) c -> p a g c", a=2))
            copied.then_inc(done[i % 2], 1)

        def empty_columns(eng, u, kind, b):
            fill = ("C", 0, b)
            bank = t_bank(kind, fill)
            eng.wait_ge(T_full[bank], t_signals(u, kind, fill) + 1)
            if b == 0:
                nc.scalar.copy(Zd[:, :, :], ET[:, :, :, 0:1].rearrange(
                    "p q (j s) f -> p s (q j f)", s=GROUP))
            if b == 1:
                nc.vector.memset(U.rearrange("p s (f k) -> p s f k", k=PITCH)[:, :, 1:F:2, HALF], 0.0)
            src = psT[bank][:, :].rearrange("p (c s f) -> p s c f", c=4, s=GROUP)
            for c in range(1 + 4 * b, min(5 + 4 * b, FEXT), 2):
                lo, hi, nc2 = max(0, c - HALF), min(F, c + 1), min(2, FEXT - c)
                start = U[:, :, lo * PITCH + c - lo - 1:lo * PITCH + c - lo]
                dst = bass.AP(tensor=start.tensor, offset=start.offset,
                              ap=[list(start.ap[0]), list(start.ap[1]), [1, nc2],
                                  [PITCH - 1, hi - lo]])
                copied = copy_out(eng, src[:, :, (c - 1) % 4:(c - 1) % 4 + nc2, lo:hi], dst)
            copied.then_inc(T_out[bank], 1)

        def empty_turned_pairs(eng, u, kind, kp):
            fill = ("K", 0, kp)
            bank = t_bank(kind, fill)
            eng.wait_ge(T_full[bank], t_signals(u, kind, fill) + 1)
            copy_out(eng, psT[bank][0:rows_of(kp), :], Zp[0:rows_of(kp), kp, :]).then_inc(T_out[bank], 1)

        def empty_part(eng, u, kind, part, v):
            bank = m_bank(kind, ("part", tile_of_part(kind, part), part))
            eng.wait_ge(L_full[part % 2], l_fills(v, part) + 1)
            if part == PARTS - 1:
                done = nc.scalar.copy(Y[:, bass.ds(v * GROUP, GROUP)], psM[bank][:, 0:GROUP])
            else:
                bias = b1s[:, part:part + 1] if part < M1 else b2s[:, part - M1:part - M1 + 1]
                dst = h1[:, part, :] if part < M1 else h2[:, part - M1, :]
                if eng is nc.scalar:
                    done = nc.scalar.activation(dst, psM[bank][:, :], ACT.Relu, bias=bias)
                else:
                    done = nc.vector.tensor_scalar(dst, psM[bank][:, :], bias, 0.0, ALU.add, ALU.max)
            done.then_inc(M_out[bank], 1)

        @block.scalar
        def _(act):
            for h in range(NS):
                act.wait_ge(table_in[h], 16)
                nc.scalar.copy(tab_hi[0:ROWS_P, h].rearrange("p k d -> p (k d)"),
                               raw_table(h)).then_inc(hi_ready, 1)

            def empty_one_hot(n, half, q0, bank, fill):
                act.wait_ge(hot_used[OH_RING - 1], hot_uses(n, FILL_CHUNKS * (fill + 1) - 1) + 1)
                f = NE + half * OH_TABLES + 2 * fill
                src = psM[bank][:, :].rearrange("p (f q n) -> p f q n", f=2, q=2)
                dst = ET[:, q0:q0 + 2].rearrange("p q n f -> p f q n")
                nc.scalar.copy(dst[:, f:f + 2], src).then_inc(M_out[bank], 1)

            def empty_tile(u, kind, q, b):
                fill = ("T", q, b)
                bank = t_bank(kind, fill)
                if b == T_BANKS - 1:
                    act.wait_ge(E_free[(q + 2) % TILES], e_freed(u, q))
                else:
                    act.wait_ge(T_full[bank], t_signals(u, kind, fill) + 1)
                nf = min(4, NE - 4 * b)
                nc.scalar.copy(
                    ET[:, q].rearrange("p n f -> p f n")[:, 4 * b:4 * b + nf],
                    psT[bank][:, 0:nf * P].rearrange("p (f n) -> p f n", f=nf),
                ).then_inc(T_out[bank], 1)

            def super_tile(u, kind, v):
                for q in tiles_of(kind):
                    for step, i in steps_of(kind, q):
                        if step == "T":
                            empty_tile(u, kind, q, i)
                        elif step == "hot" and (i + 1) % FILL_CHUNKS == 0:
                            fill = ("hot", q, i + 1 - FILL_CHUNKS)
                            empty_one_hot(hot_slot(u, q), q % 2, 2 if q < 2 else 0,
                                          m_bank(kind, fill), i // FILL_CHUNKS)
                        elif step == "gram":
                            empty_grams(nc.scalar, ACT_GRAMS, G_out_act, u, q, i)
                        elif step == "C" and i % 2 == 0:
                            empty_columns(nc.scalar, u, kind, i)
                        elif step == "K" and i % 2 == 0:
                            empty_turned_pairs(nc.scalar, u, kind, i)
                        elif step == "part" and i % 2 == 0:
                            empty_part(nc.scalar, u, kind, i, v)

            for half in range(2):
                for fill in range(OH_FILLS):
                    empty_one_hot(half, half, 0, fill % 2, fill)
            super_tile(0, FIRST, None)
            act.wait_ge(weights_in, 16 * 5)
            with act.Fori(1, LAST) as u:
                super_tile(u, MIDDLE, u - 1)
            super_tile(LAST, LAST_ONE, LAST - 1)
            super_tile(LAST, END, LAST)

        @block.vector
        def _(dve):
            nc.vector.memset(ET[:, 0:2, :, F:], 0.0).then_inc(pad_ready, 1)

            def build_one_hot(n, half, loads, chunk):
                r = chunk % OH_RING
                t, c = chunk // (ROWS_K // CHUNK_K), chunk % (ROWS_K // CHUNK_K)
                if chunk == 0:
                    dve.wait_ge(oidx_in[half], 16 * loads)
                dve.wait_ge(hot_used[r], hot_uses(n, chunk))
                ids = oidx[0:ROWS_P, half, t, :].unsqueeze(1).to_broadcast([ROWS_P, CHUNK_K, PAIR_N])
                rows = row_id[0:ROWS_P, c * CHUNK_K:(c + 1) * CHUNK_K].unsqueeze(2).to_broadcast(
                    [ROWS_P, CHUNK_K, PAIR_N])
                nc.vector.tensor_tensor(one_hot[0:ROWS_P, r], ids, rows,
                                        ALU.is_equal).then_inc(hot_full[r], 1)

            def super_tile(u, kind, v):
                for q in tiles_of(kind):
                    for step, i in steps_of(kind, q):
                        if step == "hot":
                            ahead = i + OH_RING
                            if ahead < OH_CHUNKS:
                                build_one_hot(hot_slot(u, q), q % 2, 2 * u + (q + 2) // 2 + 1, ahead)
                            elif has_hot_slot(kind, q + 1):
                                build_one_hot(hot_slot(u, q + 1), (q + 1) % 2,
                                              2 * u + (q + 3) // 2 + 1, ahead - OH_CHUNKS)
                        elif step == "gram":
                            empty_grams(nc.vector, DVE_GRAMS, G_out_dve, u, q, i)
                        elif step == "C" and i % 2 == 1:
                            empty_columns(nc.vector, u, kind, i)
                        elif step == "K" and i % 2 == 1:
                            empty_turned_pairs(nc.vector, u, kind, i)
                        elif step == "part" and i % 2 == 1:
                            empty_part(nc.vector, u, kind, i, v)

            dve.wait_ge(row_id_ready, 1)
            for h in range(NS):
                dve.wait_ge(hi_ready, h + 1)
                dve.wait_ge(table_in[h], 16)
                nc.vector.tensor_tensor(tab_lo[0:ROWS_P, h].rearrange("p k d -> p (k d)"),
                                        raw_table(h),
                                        tab_hi[0:ROWS_P, h].rearrange("p k d -> p (k d)").bitcast(f32),
                                        ALU.subtract).then_inc(lo_ready, 1)
                for c in range(ROWS_K // CHUNK_K):
                    t = h % OH_TABLES
                    build_one_hot(h // OH_TABLES, h // OH_TABLES, 1, t * (ROWS_K // CHUNK_K) + c)
            dve.wait_ge(lo_ready, NS)
            nc.vector.memset(ET[:, 2:4, :, F:], 0.0).then_inc(pad_ready, 1)
            dve.wait_ge(w1d_in, 16)
            nc.vector.tensor_tensor(w1d[:, :], raw_w1d[:, 0, :], raw_w1d[:, 1, :],
                                    ALU.add).then_inc(w1d_ready, 1)
            for chunk in range(OH_RING):
                build_one_hot(hot_slot(0, 0), 0, 2, chunk)
            super_tile(0, FIRST, None)
            dve.wait_ge(weights_in, 16 * 5)
            with dve.Fori(1, LAST) as u:
                super_tile(u, MIDDLE, u - 1)
            super_tile(LAST, LAST_ONE, LAST - 1)
            super_tile(LAST, END, LAST)


_TABLES = 26
_CHUNK = 128


def kernel(**inputs):
    import numpy as _np
    import concourse.bacc as _bacc
    from concourse import mybir as _mybir
    from concourse.bass_utils import run_bass_kernel_spmd as _run

    x = {name: _np.asarray(a) for name, a in inputs.items()}
    batch = x["ids"].shape[0]
    small = [t for t in range(_TABLES) if x[f"tbl_{t}"].shape[0] == ONE_HOT_ROWS]
    gathered = [t for t in range(_TABLES) if t not in small]
    supers = batch // 512

    ids = x["ids"].reshape(4, 32, supers, 4, _TABLES).transpose(2, 0, 1, 3, 4).reshape(4 * supers, _CHUNK, _TABLES)
    dense = x["r_dense_output"].reshape(4, 32, supers, 4, 128).transpose(2, 0, 1, 3, 4).reshape(4 * supers, _CHUNK, 128)
    by_table = ids[:, :, small].reshape(2 * supers, 2 * _CHUNK, 2, len(small) // 2)
    one_hot_idx = by_table.transpose(0, 2, 3, 1).reshape(4 * supers, len(small) // 2 * 2 * _CHUNK)

    order = [0] + [1 + t for t in gathered + small]
    F = len(order)
    first = _np.cumsum([0] + [F - 1 - a for a in range(F)])
    W1 = x["W_top1"]
    W1_pairs = _np.zeros((F, F // 2 + 1, W1.shape[1]), W1.dtype)
    for f in range(F):
        for k in range(1, F // 2 + 1):
            a, b = sorted((order[f], order[(f + k) % F]))
            W1_pairs[f, k - 1] = W1[128 + int(first[a]) + b - a - 1]
    arrays = {
        "dense": dense,
        "gather_idx": ids[:, :, gathered],
        "one_hot_idx": one_hot_idx,
        "W1_dense": _np.stack([W1[:128], W1[-128:]]),
        "W1_pairs": W1_pairs.reshape(-1, W1.shape[1]),
        "b1": x["b_top1"].reshape(-1, 128).T,
        "W2": x["W_top2"],
        "b2": x["b_top2"].reshape(-1, 128).T,
        "w3": x["W_top3"].reshape(-1, 128).T,
    }
    for t in range(_TABLES):
        arrays[f"tbl_{t}"] = x[f"tbl_{t}"]
    arrays = {name: _np.ascontiguousarray(a) for name, a in arrays.items()}

    nc = _bacc.Bacc("TRN2", target_bir_lowering=False, num_devices=1)
    aps = {name: nc.dram_tensor(name, a.shape, _mybir.dt.from_np(a.dtype), kind="ExternalInput").ap()
           for name, a in arrays.items()}
    out = nc.dram_tensor("out", (batch, 1), _mybir.dt.float32, kind="ExternalOutput").ap()
    dlrm_program(nc, aps["dense"], aps["gather_idx"], aps["one_hot_idx"],
                 [aps[f"tbl_{t}"] for t in gathered], [aps[f"tbl_{t}"] for t in small],
                 aps["W1_dense"], aps["W1_pairs"], aps["b1"], aps["W2"], aps["b2"], aps["w3"], out)
    result = _run(nc, [arrays], core_ids=[0])
    return result.results[0]["out"]
```

```python
import concourse.bass as bass
from concourse import mybir
from contextlib import ExitStack

P = 128
D = 128
GROUP = 4
SPAN = P // GROUP
TILES = 4
ONE_HOT_ROWS = 1000
ONE_HOT_TABLES = 6


def dlrm_program(nc, dense, gather_idx, one_hot_idx, gathered, small, W1_dense, W1_pairs, b1, W2,
                 b2, w3, out):
    f32, f32r, i32 = mybir.dt.float32, mybir.dt.float32r, mybir.dt.int32
    ALU = mybir.AluOpType
    ACT = mybir.ActivationFunctionType

    batch = out.shape[0]
    SUPERS = batch // (TILES * P)
    LAST = SUPERS - 1
    N = TILES * P
    PAIR_N = 2 * P
    NG = len(gathered)
    NS = len(small)
    F = 1 + NG + NS
    NE = 1 + NG
    HALF = F // 2
    FEXT = F + HALF
    F_BLOCK = 9
    PITCH = HALF + 1
    PAIR_ROWS = F_BLOCK * PITCH
    KP = F // F_BLOCK
    H1, H2 = W1_dense.shape[-1], W2.shape[-1]
    M1, M2 = H1 // P, H2 // P
    T_BANKS = -(-NE // 4)
    C_BANKS = -(-(FEXT - 1) // 4)
    GROUPS = P // GROUP
    G_SIZE = 8
    G_FILLS = GROUPS // G_SIZE
    G_COLS = GROUP * F
    ROWS_K = 8
    ROWS_P = ONE_HOT_ROWS // ROWS_K
    CHUNK_K = 4
    OH_TABLES = NS // 2
    OH_CHUNKS = OH_TABLES * ROWS_K // CHUNK_K
    OH_RING = 2
    OH_FILLS = -(-OH_TABLES // 2)

    ctx = ExitStack()
    with ctx:
        def sb(name, shape, dt):
            return ctx.enter_context(nc.sbuf_tensor(name, shape, dt))

        def pb(name, shape, dt):
            return ctx.enter_context(nc.psum_tensor(name, shape, dt))

        def sem(name):
            return ctx.enter_context(nc.semaphore(name))

        def sems(name, n):
            return [sem(f"{name}{i}") for i in range(n)]

        E = sb("E", [P, 2, NE, D], f32)
        ET = sb("ET", [P, TILES, P, SPAN], f32)
        tab_hi = sb("tab_hi", [P, NS, ROWS_K, D], f32r)
        tab_lo = sb("tab_lo", [P, NS, ROWS_K, D], f32r)
        one_hot = sb("one_hot", [P, OH_RING, CHUNK_K, PAIR_N], f32r)
        gidx = sb("gidx", [P, TILES, NG], i32)
        oidx = sb("oidx", [P, 2, OH_TABLES, PAIR_N], i32)
        row_id = sb("row_id", [P, ROWS_K], i32)
        ident = sb("ident", [P, P], f32)
        S = sb("S", [P, P, F], f32)
        UH = sb("UH", [P, M1 * N], f32)
        U = UH[:, 0:GROUP * F * PITCH].rearrange("p (s r) -> p s r", s=GROUP)
        h1 = UH[:, :].rearrange("p (m n) -> p m n", m=M1)
        Zp_hi, Zp_lo = sb("Zp_hi", [P, KP, N], f32r), sb("Zp_lo", [P, KP, N], f32r)
        w1p_hi = sb("w1p_hi", [PAIR_ROWS, KP, H1], f32r)
        w1p_lo = sb("w1p_lo", [PAIR_ROWS, KP, H1], f32r)
        Zd = sb("Zd", [P, GROUP, P], f32)
        w1d = sb("w1d", [P, H1], f32)
        h2 = sb("h2", [P, M2, N], f32)
        w2 = sb("w2", [P, M1, H2], f32)
        w3s = sb("w3s", [P, M2], f32)
        b1s = sb("b1s", [P, M1], f32)
        b2s = sb("b2s", [P, M2], f32)
        credit = sb("credit", [1, 2], f32)
        Y = sb("Y", [P, SUPERS * GROUP], f32)

        psT = [pb(f"psT{i}", [P, 512], f32) for i in range(2)]
        psM = [pb(f"psM{i}", [P, 512], f32) for i in range(2)]
        psG = [pb(f"psG{i}", [P, 2, 512], f32) for i in range(2)]

        raw_tables = ET[:, 2:4].rearrange("p q n f -> p (q n f)")

        def raw_table(h):
            return raw_tables[0:ROWS_P, h * ROWS_K * D:(h + 1) * ROWS_K * D]

        raw_w1p = UH[0:PAIR_ROWS, 0:KP * H1].rearrange("p (k n) -> p k n", k=KP)
        raw_w1d = S[:, P // 2:, :].rearrange("p j f -> p (j f)")[:, 0:2 * H1].rearrange(
            "p (a n) -> p a n", a=2)

        gidx_in = sems("gidx_in", TILES)
        dense_in = sems("dense_in", 2)
        oidx_in = sems("oidx_in", 2)
        table_in = sems("table_in", NS)
        w1_in, weights_in = sem("w1_in"), sem("weights_in")
        gathered_in = [sems(f"gathered_in{i}_", T_BANKS) for i in range(2)]
        zeroed, ident_ready, row_id_ready = sem("zeroed"), sem("ident_ready"), sem("row_id_ready")
        pad_ready, hi_ready = sem("pad_ready"), sem("hi_ready")
        w1d_ready, w1_hi_ready, w1_lo_ready = sem("w1d_ready"), sem("w1_hi_ready"), sem("w1_lo_ready")
        lo_ready = sem("lo_ready")
        Zd_ready, Zp_hi_ready = sem("Zd_ready"), sem("Zp_hi_ready")
        E_free = sems("E_free", TILES)
        T_full = sems("T_full", 2)
        T_out = sems("T_out", 2)
        M_out = sems("M_out", 2)
        L_full = sems("L_full", 2)
        G_full = sems("G_full", 2)
        G_out_act, G_out_dve = sems("G_out_act", 2), sems("G_out_dve", 2)
        hot_full, hot_used = sems("hot_full", OH_RING), sems("hot_used", OH_RING)

        def e_freed(u, q):
            return 16 * (u + 1 + (q + 2) // TILES)

        FIRST, MIDDLE, LAST_ONE, END = range(4)
        PARTS = M1 + M2 + 1
        FILL_CHUNKS = 2 * ROWS_K // CHUNK_K

        AHEAD = (0, 1)

        def has_hot_slot(kind, q):
            return not (kind == LAST_ONE and q >= 2)

        def between(steps, inserted, every=1):
            merged = []
            for i, step in enumerate(steps):
                merged.append(step)
                if (i + 1) % every == 0 and inserted:
                    merged.append(inserted[0])
                    inserted = inserted[1:]
            return merged + inserted

        def steps_of(kind, q):
            columns, pairs = [("C", b) for b in range(C_BANKS)], [("K", k) for k in range(KP)]
            if kind == END:
                return [("D", AHEAD[1])] + columns + pairs + [("part", p) for p in range(PARTS)]
            tile = [("T", b) for b in range(T_BANKS)]
            hot = [("hot", c) for c in range(OH_CHUNKS)] if has_hot_slot(kind, q) else []
            grams = [("gram", i) for i in range(G_FILLS)]
            parts = [("part", p) for p in range(2 * q, min(2 * q + 2, PARTS))]
            if kind == FIRST:
                return between(tile, hot[:T_BANKS - 1]) + between(hot[T_BANKS - 1:], grams)
            if q == 0:
                half = C_BANKS // 2
                return ([("Z", 0)] + hot[:1] + columns[:half] + hot[1:2] + columns[half:] +
                        between(tile, hot[2:5], 2) + hot[5:] + pairs[:2] + grams[:1] + pairs[2:] +
                        grams[1:2] + between(parts, grams[2:]))
            first, second = hot[:FILL_CHUNKS], hot[FILL_CHUNKS:]
            if not hot:
                if q < TILES - 1:
                    return between(tile, parts[:1], T_BANKS - 2) + parts[1:] + grams
                return tile[:-2] + [("Z", 1)] + parts + tile[-2:] + [("D", AHEAD[0])] + grams
            return between(tile, first, 2) + between(parts, second[:1]) + between(grams, second[1:])

        def tiles_of(kind):
            return range(1 if kind == END else TILES)

        def T_fills(kind):
            return [(step, q, i) for q in tiles_of(kind) for step, i in steps_of(kind, q)
                    if step in ("T", "C", "K")]

        def M_fills(kind):
            return [(step, q, i) for q in tiles_of(kind) for step, i in steps_of(kind, q)
                    if step == "part" or (step == "hot" and i % FILL_CHUNKS == 0)]

        def bank_of(fills, kind, fill):
            return fills(kind).index(fill) % 2

        def signals_T_full(fill):
            return fill[0] != "T" or fill[2] < T_BANKS - 1

        def fills_before(fills, u, kind, fill, counted=lambda fill: True):
            i = fills(kind).index(fill)

            def count(sequence):
                return sum(1 for other in sequence[i % 2::2] if counted(other))

            before = 0
            if kind != FIRST:
                before = count(fills(FIRST)) + (u - 1) * count(fills(MIDDLE))
            if kind == END:
                before = before + count(fills(LAST_ONE))
            return before + count(fills(kind)[:i])

        def t_bank(kind, fill):
            return bank_of(T_fills, kind, fill)

        def t_uses(u, kind, fill):
            return fills_before(T_fills, u, kind, fill)

        def t_signals(u, kind, fill):
            return fills_before(T_fills, u, kind, fill, signals_T_full)

        def m_bank(kind, fill):
            return bank_of(M_fills, kind, fill)

        def m_uses(u, kind, fill):
            return OH_FILLS + fills_before(M_fills, u, kind, fill)

        def tile_of_part(kind, part):
            return 0 if kind == END else part // 2

        def l_fills(v, part):
            return (PARTS + 1 - part % 2) // 2 * v + part // 2

        def g_uses(u, q, i):
            return (TILES * u + q) * (G_FILLS // 2) + i // 2

        def hot_uses(n, c):
            return n * (OH_CHUNKS // OH_RING) + c // OH_RING

        def hot_slot(u, q):
            return TILES * u + q + 2

        def rows_of(kp):
            return PAIR_ROWS - (1 if kp == KP - 1 else 0)

        block = ctx.enter_context(nc.Block())

        @block.gpsimd
        def _(pool):
            nc.gpsimd.iota(row_id[:, :], pattern=[[1, ROWS_K]], base=0,
                           channel_multiplier=ROWS_K).then_inc(row_id_ready, 1)
            nc.gpsimd.memset(ident[:, :], 0.0).then_inc(zeroed, 1)
            for q in range(2):
                nc.gpsimd.memset(credit[:, q:q + 1], 0.0).then_inc(E_free[q], 16)
            pool.wait_ge(zeroed, 1)
            nc.gpsimd.affine_select(out=ident[:, :], in_=ident[:, :], compare_op=ALU.not_equal,
                                    fill=1.0, base=0, pattern=[[-1, P]],
                                    channel_multiplier=1).then_inc(ident_ready, 1)

            def super_tile(loads):
                for q in range(TILES):
                    pool.wait_ge(ident_ready, 1)
                    pool.wait_ge(gidx_in[q], loads)
                    pool.wait_ge(E_free[q], loads)
                    for g in range(NG):
                        pool.indirect_dma_start(
                            E[:, q % 2, 1 + g, :], None, gathered[g],
                            bass.IndirectOffsetOnAxis(ap=gidx[:, q, g:g + 1], axis=0),
                        ).then_inc(gathered_in[q % 2][(1 + g) // 4], 16)

            with pool.Fori(16, 16 * (SUPERS + 1), 16) as loads:
                super_tile(loads)

        @block.sync
        def _(sp):
            def load_gidx(u, q):
                sp.dma_start(gidx[:, q, :], gather_idx[u * TILES + q]).then_inc(gidx_in[q], 16)

            def load_dense(tile, slot):
                sp.dma_start(E[:, slot, 0, :], dense[tile]).then_inc(dense_in[slot], 16)

            def load_oidx(n, half):
                sp.dma_start(oidx[:, half].rearrange("p t n -> p (t n)"),
                             one_hot_idx[n].partition_broadcast(P)).then_inc(oidx_in[half], 16)

            load_gidx(0, 0)
            load_oidx(0, 0)
            for h in range(NS):
                sp.dma_start(raw_table(h), small[h].rearrange("(p k) d -> p (k d)", k=ROWS_K)
                             ).then_inc(table_in[h], 16)
                if h == 0:
                    for q in range(1, TILES):
                        load_gidx(0, q)
                    load_dense(0, 0)
                    load_dense(1, 1)
                    load_oidx(1, 1)
            sp.dma_start(raw_w1d, W1_dense.rearrange("a p n -> p a n")).then_inc(w1_in, 16)
            sp.dma_start(raw_w1p, W1_pairs.rearrange("(k p) n -> p k n", k=KP)).then_inc(w1_in, 16)
            sp.dma_start(w2[:, :, :], W2.rearrange("(k p) n -> p k n", p=P)).then_inc(weights_in, 16)
            sp.dma_start(b1s[:, :], b1).then_inc(weights_in, 16)
            sp.dma_start(b2s[:, :], b2).then_inc(weights_in, 16)
            sp.dma_start(w3s[:, :], w3).then_inc(weights_in, 16)

            sp.wait_ge(hot_full[OH_RING - 1], hot_uses(1, 0))
            load_oidx(2, 0)

            def super_tile(u, kind):
                for q in range(TILES):
                    if has_hot_slot(kind, q + 1):
                        sp.wait_ge(hot_full[OH_RING - 1], hot_uses(hot_slot(u, q), 0))
                        load_oidx(hot_slot(u, q) + 1, (q + 1) % 2)
                    if not (kind == LAST_ONE and q >= 2):
                        sp.wait_ge(E_free[(q + 2) % TILES], e_freed(u, q))
                        if kind != LAST_ONE:
                            load_gidx(u + 1, q)
                        load_dense(TILES * u + q + 2, q % 2)

            with sp.Fori(0, LAST) as u:
                super_tile(u, MIDDLE)
            super_tile(LAST, LAST_ONE)
            y_fill = ("part", 0, PARTS - 1)
            sp.wait_ge(M_out[m_bank(END, y_fill)], m_uses(LAST, END, y_fill) + 1)
            sp.dma_start(out.rearrange("(p c) o -> p (c o)", p=P), Y[:, :]).then_inc(weights_in, 16)
            sp.wait_ge(weights_in, 16 * 5)

        @block.tensor
        def _(pe):
            def one_hot_chunk(n, half, chunk, bank, uses):
                if chunk % FILL_CHUNKS == 0:
                    pe.wait_ge(M_out[bank], uses)
                r = chunk % OH_RING
                t, c = chunk // (ROWS_K // CHUNK_K), chunk % (ROWS_K // CHUNK_K)
                pe.wait_ge(hot_full[r], hot_uses(n, chunk) + 1)
                for kc in range(CHUNK_K):
                    k = c * CHUNK_K + kc
                    for tab in (tab_hi, tab_lo):
                        product = nc.tensor.matmul(
                            psM[bank][:, t % 2 * PAIR_N:(t % 2 + 1) * PAIR_N],
                            tab[0:ROWS_P, half * OH_TABLES + t, k, :],
                            one_hot[0:ROWS_P, r, kc, :],
                            start=(k == 0 and tab is tab_hi),
                            stop=(k == ROWS_K - 1 and tab is tab_lo))
                product.then_inc(hot_used[r], 1)

            def transpose_tile(u, kind, q, b):
                if b == 0:
                    pe.wait_ge(dense_in[q % 2], 16 * (2 * u + q // 2 + 1))
                tables = min(4 * b + 3, NG) - max(4 * b - 1, 0)
                pe.wait_ge(gathered_in[q % 2][b], 16 * tables * (2 * u + q // 2 + 1))
                fill = ("T", q, b)
                bank = t_bank(kind, fill)
                pe.wait_ge(T_out[bank], t_uses(u, kind, fill))
                for f in range(4 * b, min(4 * b + 4, NE)):
                    turned = nc.tensor.transpose(psT[bank][:, (f % 4) * P:(f % 4 + 1) * P],
                                                 E[:, q % 2, f, :], ident[:, :])
                if b == T_BANKS - 1:
                    turned.then_inc(E_free[(q + 2) % TILES], 16)
                else:
                    turned.then_inc(T_full[bank], 1)

            def wait_ET(u, kind, q):
                for fill in (("T", q, T_BANKS - 2), ("T", q, T_BANKS - 1)):
                    pe.wait_ge(T_out[t_bank(kind, fill)], t_uses(u, kind, fill) + 1)
                if q == 0:
                    for fill in M_fills(kind)[0:2]:
                        pe.wait_ge(M_out[m_bank(kind, fill)], m_uses(u, kind, fill))
                if q == 2:
                    if kind == FIRST:
                        pe.wait_ge(pad_ready, 2)
                    for fill in [fill for fill in M_fills(kind) if fill[1] == 1][-2:]:
                        pe.wait_ge(M_out[m_bank(kind, fill)], m_uses(u, kind, fill) + 1)

            def gram_fill(u, q, i):
                pe.wait_ge(G_out_act[i % 2], g_uses(u, q, i))
                pe.wait_ge(G_out_dve[i % 2], g_uses(u, q, i))
                for g in range(G_SIZE):
                    j = i * G_SIZE + g
                    four = ET[:, q, j * GROUP:(j + 1) * GROUP]
                    gram = nc.tensor.matmul(
                        psG[i % 2][:, g // 4, (g % 4) * G_COLS:(g % 4 + 1) * G_COLS],
                        four.rearrange("p s f -> p (s f)"), four[:, :, 0:F],
                        start=True, stop=True)
                gram.then_inc(G_full[i % 2], 1)

            def turn_columns(u, kind, b, v):
                if b == 0:
                    for i in range(2):
                        pe.wait_ge(G_out_act[i], g_uses(v, TILES, i))
                        pe.wait_ge(G_out_dve[i], g_uses(v, TILES, i))
                fill = ("C", 0, b)
                bank = t_bank(kind, fill)
                pe.wait_ge(T_out[bank], t_uses(u, kind, fill))
                for c in range(1 + 4 * b, min(5 + 4 * b, FEXT)):
                    turned = nc.tensor.transpose(psT[bank][:, (c - 1) % 4 * P:((c - 1) % 4 + 1) * P],
                                                 S[:, :, c % F], ident[:, :])
                turned.then_inc(T_full[bank], 1)

            def turn_pairs(u, kind, kp):
                if kp == 0:
                    for fill in (("C", 0, C_BANKS - 2), ("C", 0, C_BANKS - 1)):
                        pe.wait_ge(T_out[t_bank(kind, fill)], t_uses(u, kind, fill) + 1)
                fill = ("K", 0, kp)
                bank = t_bank(kind, fill)
                pe.wait_ge(T_out[bank], t_uses(u, kind, fill))
                for s in range(GROUP):
                    turned = nc.tensor.transpose(
                        psT[bank][0:rows_of(kp), s * P:(s + 1) * P],
                        U[:, s, kp * PAIR_ROWS:kp * PAIR_ROWS + rows_of(kp)], ident[:, :])
                turned.then_inc(T_full[bank], 1)

            def dense_product(u, kind, part, v):
                fill = ("part", tile_of_part(kind, part), part)
                bank = m_bank(kind, fill)
                pe.wait_ge(M_out[bank], m_uses(u, kind, fill))
                if part == 0:
                    pe.wait_ge(Zd_ready, v + 1)
                nc.tensor.matmul(psM[bank][:, :], w1d[:, part * P:(part + 1) * P], Zd[:, :, :],
                                 start=True, stop=False)

            def perceptron_part(u, kind, part, v):
                fill = ("part", tile_of_part(kind, part), part)
                bank = m_bank(kind, fill)
                if part < M1:
                    if not (kind == END and part in AHEAD):
                        dense_product(u, kind, part, v)
                else:
                    pe.wait_ge(M_out[bank], m_uses(u, kind, fill))

                def written(other):
                    earlier = ("part", tile_of_part(kind, other), other)
                    if m_bank(kind, earlier) != bank:
                        pe.wait_ge(M_out[1 - bank], m_uses(u, kind, earlier) + 1)

                if part < M1:
                    cols = slice(part * P, (part + 1) * P)
                    for kp in range(KP):
                        rows = slice(0, rows_of(kp))
                        if part == 0:
                            turned = ("K", 0, kp)
                            pe.wait_ge(T_out[t_bank(kind, turned)], t_uses(u, kind, turned) + 1)
                        for w, z in ((w1p_hi, Zp_hi), (w1p_hi, Zp_lo), (w1p_lo, Zp_hi)):
                            layer = nc.tensor.matmul(psM[bank][:, :], w[rows, kp, cols], z[rows, kp, :],
                                                     start=False, stop=(kp == KP - 1 and w is w1p_lo))
                elif part < M1 + M2:
                    cols = slice((part - M1) * P, (part - M1 + 1) * P)
                    for k in range(M1):
                        if part == M1:
                            written(k)
                        layer = nc.tensor.matmul(psM[bank][:, :], w2[:, k, cols], h1[:, k, :],
                                                 start=(k == 0), stop=(k == M1 - 1))
                else:
                    for k in range(M2):
                        written(M1 + k)
                    for s in range(GROUP):
                        for k in range(M2):
                            layer = nc.tensor.matmul(psM[bank][:, s:s + 1], h2[:, k, s * P:(s + 1) * P],
                                                     w3s[:, k:k + 1], start=(k == 0), stop=(k == M2 - 1))
                layer.then_inc(L_full[part % 2], 1)

            def super_tile(u, kind, v):
                for q in tiles_of(kind):
                    for step, i in steps_of(kind, q):
                        if step == "T":
                            transpose_tile(u, kind, q, i)
                        elif step == "hot":
                            fill = ("hot", q, i - i % FILL_CHUNKS)
                            one_hot_chunk(hot_slot(u, q), q % 2, i, m_bank(kind, fill),
                                          m_uses(u, kind, fill))
                        elif step == "gram":
                            if i == 0:
                                wait_ET(u, kind, q)
                            gram_fill(u, q, i)
                        elif step == "C":
                            turn_columns(u, kind, i, v)
                        elif step == "K":
                            turn_pairs(u, kind, i)
                        elif step == "D":
                            dense_product(LAST, END, i, LAST)
                        elif step == "part":
                            perceptron_part(u, kind, i, v)

            pe.wait_ge(ident_ready, 1)
            for half in range(2):
                for chunk in range(OH_CHUNKS):
                    if chunk % (ROWS_K // CHUNK_K) == 0:
                        pe.wait_ge(lo_ready, half * OH_TABLES + chunk // (ROWS_K // CHUNK_K) + 1)
                    one_hot_chunk(half, half, chunk, chunk // FILL_CHUNKS % 2, half)
            pe.wait_ge(pad_ready, 1)
            super_tile(0, FIRST, None)
            pe.wait_ge(weights_in, 16 * 4)
            pe.wait_ge(w1d_ready, 1)
            pe.wait_ge(w1_lo_ready, 1)
            with pe.Fori(1, LAST) as u:
                super_tile(u, MIDDLE, u - 1)
            super_tile(LAST, LAST_ONE, LAST - 1)
            super_tile(LAST, END, LAST)

        def dve_has_column(kind, b):
            return b % 2 == 1 and (kind == END or b < C_BANKS // 2)

        def copy_out(eng, psum, sbuf):
            return nc.scalar.copy(sbuf, psum) if eng is nc.scalar else nc.vector.tensor_copy(sbuf, psum)

        ACT_GRAMS, DVE_GRAMS = (0, 1), (2, 3)

        def empty_grams(eng, mine, done, u, q, i):
            eng.wait_ge(G_full[i % 2], g_uses(u, q, i) + 1)
            for s in mine:
                rows = slice(s * SPAN, (s + 1) * SPAN)
                blocks = psG[i % 2][rows, :, 0:4 * G_COLS].rearrange(
                    "p a (g c) -> p a g c", g=4)[:, :, :, s * F:(s + 1) * F]
                j0 = q * GROUPS + i * G_SIZE
                copied = copy_out(eng, blocks, S[rows, j0:j0 + G_SIZE, :].rearrange(
                    "p (a g) c -> p a g c", a=2))
            copied.then_inc(done[i % 2], 1)

        def empty_columns(eng, u, kind, b):
            fill = ("C", 0, b)
            bank = t_bank(kind, fill)
            eng.wait_ge(T_full[bank], t_signals(u, kind, fill) + 1)
            if b == 1:
                nc.vector.memset(U.rearrange("p s (f k) -> p s f k", k=PITCH)[:, :, 1:F:2, HALF], 0.0)
            src = psT[bank][:, :].rearrange("p (c s f) -> p s c f", c=4, s=GROUP)
            for c in range(1 + 4 * b, min(5 + 4 * b, FEXT), 2):
                lo, hi, nc2 = max(0, c - HALF), min(F, c + 1), min(2, FEXT - c)
                start = U[:, :, lo * PITCH + c - lo - 1:lo * PITCH + c - lo]
                dst = bass.AP(tensor=start.tensor, offset=start.offset,
                              ap=[list(start.ap[0]), list(start.ap[1]), [1, nc2],
                                  [PITCH - 1, hi - lo]])
                copied = copy_out(eng, src[:, :, (c - 1) % 4:(c - 1) % 4 + nc2, lo:hi], dst)
            copied.then_inc(T_out[bank], 1)

        def empty_part(eng, u, kind, part, v):
            bank = m_bank(kind, ("part", tile_of_part(kind, part), part))
            eng.wait_ge(L_full[part % 2], l_fills(v, part) + 1)
            if part == PARTS - 1:
                done = nc.scalar.copy(Y[:, bass.ds(v * GROUP, GROUP)], psM[bank][:, 0:GROUP])
            else:
                bias = b1s[:, part:part + 1] if part < M1 else b2s[:, part - M1:part - M1 + 1]
                dst = h1[:, part, :] if part < M1 else h2[:, part - M1, :]
                if eng is nc.scalar:
                    done = nc.scalar.activation(dst, psM[bank][:, :], ACT.Relu, bias=bias)
                else:
                    done = nc.vector.tensor_scalar(dst, psM[bank][:, :], bias, 0.0, ALU.add, ALU.max)
            done.then_inc(M_out[bank], 1)

        @block.scalar
        def _(act):
            for h in range(NS):
                act.wait_ge(table_in[h], 16)
                nc.scalar.copy(tab_hi[0:ROWS_P, h].rearrange("p k d -> p (k d)"),
                               raw_table(h)).then_inc(hi_ready, 1)

            def empty_one_hot(n, half, q0, bank, fill):
                last = min(FILL_CHUNKS * (fill + 1), OH_CHUNKS) - 1
                act.wait_ge(hot_used[last % OH_RING], hot_uses(n, last) + 1)
                f, nf = NE + half * OH_TABLES + 2 * fill, min(2, OH_TABLES - 2 * fill)
                src = psM[bank][:, 0:nf * PAIR_N].rearrange("p (f q n) -> p f q n", f=nf, q=2)
                dst = ET[:, q0:q0 + 2].rearrange("p q n f -> p f q n")
                nc.scalar.copy(dst[:, f:f + nf], src).then_inc(M_out[bank], 1)

            def empty_tile(u, kind, q, b):
                fill = ("T", q, b)
                bank = t_bank(kind, fill)
                if b == T_BANKS - 1:
                    act.wait_ge(E_free[(q + 2) % TILES], e_freed(u, q))
                else:
                    act.wait_ge(T_full[bank], t_signals(u, kind, fill) + 1)
                nf = min(4, NE - 4 * b)
                nc.scalar.copy(
                    ET[:, q].rearrange("p n f -> p f n")[:, 4 * b:4 * b + nf],
                    psT[bank][:, 0:nf * P].rearrange("p (f n) -> p f n", f=nf),
                ).then_inc(T_out[bank], 1)

            ends_of_fills = [min(FILL_CHUNKS * (fill + 1), OH_CHUNKS) - 1 for fill in range(OH_FILLS)]

            def round_W1():
                act.wait_ge(w1_in, 16 * 2)
                nc.scalar.copy(w1p_hi[:, :, :], raw_w1p).then_inc(w1_hi_ready, 1)

            def super_tile(u, kind, v):
                for q in tiles_of(kind):
                    if kind == FIRST and q == 1:
                        round_W1()
                    for step, i in steps_of(kind, q):
                        if step == "T":
                            if kind != FIRST and q == 0 and i == 0:
                                act.wait_ge(Zd_ready, v + 1)
                            empty_tile(u, kind, q, i)
                        elif step == "hot" and i in ends_of_fills:
                            fill = ("hot", q, i - i % FILL_CHUNKS)
                            empty_one_hot(hot_slot(u, q), q % 2, 2 if q < 2 else 0,
                                          m_bank(kind, fill), i // FILL_CHUNKS)
                        elif step == "gram":
                            empty_grams(nc.scalar, ACT_GRAMS, G_out_act, u, q, i)
                        elif step == "Z":
                            nc.scalar.copy(Zd[:, :, :], ET[:, :, :, 0:1].rearrange(
                                "p q (j s) f -> p s (q j f)", s=GROUP)).then_inc(Zd_ready, 1)
                        elif step == "C" and not dve_has_column(kind, i):
                            empty_columns(nc.scalar, u, kind, i)
                        elif step == "K":
                            fill = ("K", 0, i)
                            bank, rows = t_bank(kind, fill), rows_of(i)
                            act.wait_ge(T_full[bank], t_signals(u, kind, fill) + 1)
                            nc.scalar.copy(Zp_hi[0:rows, i, :], psT[bank][0:rows, :]).then_inc(Zp_hi_ready, 1)
                        elif step == "part" and i % 2 == 0:
                            empty_part(nc.scalar, u, kind, i, v)

            for half in range(2):
                for fill in range(OH_FILLS):
                    empty_one_hot(half, half, 0, fill % 2, fill)
            super_tile(0, FIRST, None)
            act.wait_ge(weights_in, 16 * 4)
            with act.Fori(1, LAST) as u:
                super_tile(u, MIDDLE, u - 1)
            super_tile(LAST, LAST_ONE, LAST - 1)
            super_tile(LAST, END, LAST)

        @block.vector
        def _(dve):
            nc.vector.memset(ET[:, 0:2, :, F:], 0.0).then_inc(pad_ready, 1)

            def build_one_hot(n, half, loads, chunk):
                r = chunk % OH_RING
                t, c = chunk // (ROWS_K // CHUNK_K), chunk % (ROWS_K // CHUNK_K)
                if chunk == 0:
                    dve.wait_ge(oidx_in[half], 16 * loads)
                dve.wait_ge(hot_used[r], hot_uses(n, chunk))
                ids = oidx[0:ROWS_P, half, t, :].unsqueeze(1).to_broadcast([ROWS_P, CHUNK_K, PAIR_N])
                rows = row_id[0:ROWS_P, c * CHUNK_K:(c + 1) * CHUNK_K].unsqueeze(2).to_broadcast(
                    [ROWS_P, CHUNK_K, PAIR_N])
                nc.vector.tensor_tensor(one_hot[0:ROWS_P, r], ids, rows,
                                        ALU.is_equal).then_inc(hot_full[r], 1)

            def split_W1():
                dve.wait_ge(w1_in, 16 * 2)
                nc.vector.tensor_tensor(w1d[:, :], raw_w1d[:, 0, :], raw_w1d[:, 1, :],
                                        ALU.add).then_inc(w1d_ready, 1)
                dve.wait_ge(w1_hi_ready, 1)
                nc.vector.tensor_tensor(w1p_lo[:, :, :], raw_w1p, w1p_hi[:, :, :].bitcast(f32),
                                        ALU.subtract).then_inc(w1_lo_ready, 1)

            def super_tile(u, kind, v):
                for q in tiles_of(kind):
                    if kind == FIRST and q == 1:
                        split_W1()
                    for step, i in steps_of(kind, q):
                        if step == "hot":
                            ahead = i + OH_RING
                            if ahead < OH_CHUNKS:
                                build_one_hot(hot_slot(u, q), q % 2, 2 * u + (q + 2) // 2 + 1, ahead)
                            elif has_hot_slot(kind, q + 1):
                                build_one_hot(hot_slot(u, q + 1), (q + 1) % 2,
                                              2 * u + (q + 3) // 2 + 1, ahead - OH_CHUNKS)
                        elif step == "gram":
                            empty_grams(nc.vector, DVE_GRAMS, G_out_dve, u, q, i)
                        elif step == "C" and dve_has_column(kind, i):
                            empty_columns(nc.vector, u, kind, i)
                        elif step == "K":
                            bank, rows = t_bank(kind, ("K", 0, i)), rows_of(i)
                            dve.wait_ge(Zp_hi_ready, KP * v + i + 1)
                            nc.vector.tensor_tensor(Zp_lo[0:rows, i, :], psT[bank][0:rows, :],
                                                    Zp_hi[0:rows, i, :].bitcast(f32),
                                                    ALU.subtract).then_inc(T_out[bank], 1)
                        elif step == "part" and i % 2 == 1:
                            empty_part(nc.vector, u, kind, i, v)

            def build_tables_rows(h):
                per = ROWS_K // CHUNK_K
                for c in range(per):
                    build_one_hot(h // OH_TABLES, h // OH_TABLES, 1, h % OH_TABLES * per + c)

            dve.wait_ge(row_id_ready, 1)
            build_tables_rows(0)
            for h in range(NS):
                dve.wait_ge(hi_ready, h + 1)
                dve.wait_ge(table_in[h], 16)
                nc.vector.tensor_tensor(tab_lo[0:ROWS_P, h].rearrange("p k d -> p (k d)"),
                                        raw_table(h),
                                        tab_hi[0:ROWS_P, h].rearrange("p k d -> p (k d)").bitcast(f32),
                                        ALU.subtract).then_inc(lo_ready, 1)
                if h > 0:
                    build_tables_rows(h)
            for chunk in range(OH_RING):
                build_one_hot(hot_slot(0, 0), 0, 2, chunk)
            dve.wait_ge(lo_ready, NS)
            nc.vector.memset(ET[:, 2:4, :, F:], 0.0).then_inc(pad_ready, 1)
            super_tile(0, FIRST, None)
            dve.wait_ge(weights_in, 16 * 4)
            with dve.Fori(1, LAST) as u:
                super_tile(u, MIDDLE, u - 1)
            super_tile(LAST, LAST_ONE, LAST - 1)
            super_tile(LAST, END, LAST)


_TABLES = 26


def kernel(**inputs):
    import numpy as _np
    import concourse.bacc as _bacc
    from concourse import mybir as _mybir
    from concourse.bass_utils import run_bass_kernel_spmd as _run

    x = {name: _np.asarray(a) for name, a in inputs.items()}
    batch = x["ids"].shape[0]
    small = [t for t in range(_TABLES) if x[f"tbl_{t}"].shape[0] == ONE_HOT_ROWS][:ONE_HOT_TABLES]
    gathered = [t for t in range(_TABLES) if t not in small]
    supers = batch // 512

    ids = x["ids"].reshape(4, 32, supers, 4, _TABLES).transpose(2, 0, 1, 3, 4).reshape(4 * supers, P, _TABLES)
    dense = x["r_dense_output"].reshape(4, 32, supers, 4, 128).transpose(2, 0, 1, 3, 4).reshape(4 * supers, P, 128)
    by_table = ids[:, :, small].reshape(2 * supers, 2 * P, 2, len(small) // 2)
    one_hot_idx = by_table.transpose(0, 2, 3, 1).reshape(4 * supers, len(small) // 2 * 2 * P)

    order = [0] + [1 + t for t in gathered + small]
    F = len(order)
    first = _np.cumsum([0] + [F - 1 - a for a in range(F)])
    W1 = x["W_top1"]
    W1_pairs = _np.zeros((F, F // 2 + 1, W1.shape[1]), W1.dtype)
    for f in range(F):
        for k in range(1, F // 2 + 1):
            a, b = sorted((order[f], order[(f + k) % F]))
            W1_pairs[f, k - 1] = W1[128 + int(first[a]) + b - a - 1]
    arrays = {
        "dense": dense,
        "gather_idx": ids[:, :, gathered],
        "one_hot_idx": one_hot_idx,
        "W1_dense": _np.stack([W1[:128], W1[-128:]]),
        "W1_pairs": W1_pairs.reshape(-1, W1.shape[1]),
        "b1": x["b_top1"].reshape(-1, 128).T,
        "W2": x["W_top2"],
        "b2": x["b_top2"].reshape(-1, 128).T,
        "w3": x["W_top3"].reshape(-1, 128).T,
    }
    for t in range(_TABLES):
        arrays[f"tbl_{t}"] = x[f"tbl_{t}"]
    arrays = {name: _np.ascontiguousarray(a) for name, a in arrays.items()}

    nc = _bacc.Bacc("TRN2", target_bir_lowering=False, num_devices=1)
    aps = {name: nc.dram_tensor(name, a.shape, _mybir.dt.from_np(a.dtype), kind="ExternalInput").ap()
           for name, a in arrays.items()}
    out = nc.dram_tensor("out", (batch, 1), _mybir.dt.float32, kind="ExternalOutput").ap()
    dlrm_program(nc, aps["dense"], aps["gather_idx"], aps["one_hot_idx"],
                 [aps[f"tbl_{t}"] for t in gathered], [aps[f"tbl_{t}"] for t in small],
                 aps["W1_dense"], aps["W1_pairs"], aps["b1"], aps["W2"], aps["b2"], aps["w3"], out)
    result = _run(nc, [arrays], core_ids=[0])
    return result.results[0]["out"]
```
